# Optimizing a Trainium2 kernel written in Bass

```python
import numpy as np
import jax
import jax.numpy as jnp

def _softmax(x, axis=-1):
    return jax.nn.softmax(x, axis=axis)

def _gelu(x):
    return jax.nn.gelu(x, approximate=True)

def _silu(x):
    return jax.nn.silu(x)

def _sigmoid(x):
    return jax.nn.sigmoid(x)

def _layernorm(x, axis=-1, eps=1e-05):
    m = jnp.mean(x, axis=axis, keepdims=True)
    v = jnp.var(x, axis=axis, keepdims=True)
    return (x - m) / jnp.sqrt(v + eps)

def _scatter_add(tgt, idx, src, axis=0):
    return tgt.at[idx].add(src)

def _segment_sum(src, seg, n):
    return jax.ops.segment_sum(src, seg, n)
kernel_name = 'mk_rec_standalone_d1_rec_r8_6b59be'

def setup_inputs(seed: int=0):
    np.random.seed(seed)
    _w = jnp.asarray

    def _rec_inputs():
        import jax
        import jax.numpy as jnp
        _rk = jax.random.key(seed)
        r_user = jax.random.randint(jax.random.fold_in(_rk, 1), (2048,), 72, 499949, jnp.int32)
        r_item = jax.random.randint(jax.random.fold_in(_rk, 2), (2048,), 13, 99986, jnp.int32)
        return (r_user, r_item)
    r_user, r_item = _rec_inputs()

    def _L0_rec_setup():
        import jax, jax.numpy as jnp
        import numpy as np
        B = 2048
        USER_NUM = 62500
        ITEM_NUM = 12500
        D = 512
        DEEP = [512, 256, 128, 64]
        key = jax.random.key(seed)
        ks = jax.random.split(key, 12)
        s = 0.02
        inp = {'user': jax.random.randint(ks[0], (B,), 0, USER_NUM, dtype=jnp.int64 if jax.config.jax_enable_x64 else jnp.int32), 'item': jax.random.randint(ks[1], (B,), 0, ITEM_NUM, dtype=jnp.int64 if jax.config.jax_enable_x64 else jnp.int32), 'user_emb': jax.random.normal(ks[2], (USER_NUM, D // 2), dtype=jnp.float32) * s, 'item_emb': jax.random.normal(ks[3], (ITEM_NUM, D // 2), dtype=jnp.float32) * s, 'cw1': jax.random.normal(ks[4], (D,), dtype=jnp.float32) * s, 'cw2': jax.random.normal(ks[5], (D,), dtype=jnp.float32) * s, 'dW1': jax.random.normal(ks[6], (DEEP[0], DEEP[1]), dtype=jnp.float32) * s, 'db1': jnp.zeros((DEEP[1],), dtype=jnp.float32), 'dW2': jax.random.normal(ks[7], (DEEP[1], DEEP[2]), dtype=jnp.float32) * s, 'db2': jnp.zeros((DEEP[2],), dtype=jnp.float32), 'dW3': jax.random.normal(ks[8], (DEEP[2], DEEP[3]), dtype=jnp.float32) * s, 'db3': jnp.zeros((DEEP[3],), dtype=jnp.float32), 'Wo': jax.random.normal(ks[9], (D + DEEP[3], 1), dtype=jnp.float32) * s, 'bo': jnp.zeros((1,), dtype=jnp.float32)}
        return inp
    _L0_rec_all = _L0_rec_setup()
    _L0_rec_in = {k: v for k, v in _L0_rec_all.items() if k in ('user_emb', 'item_emb', 'cw1', 'cw2', 'dW1', 'db1', 'dW2', 'db2', 'dW3', 'db3', 'Wo', 'bo')}
    del _L0_rec_all
    return {'r_user': r_user, 'r_item': r_item, 'L0_rec_user_emb': _L0_rec_in['user_emb'], 'L0_rec_item_emb': _L0_rec_in['item_emb'], 'L0_rec_cw1': _L0_rec_in['cw1'], 'L0_rec_cw2': _L0_rec_in['cw2'], 'L0_rec_dW1': _L0_rec_in['dW1'], 'L0_rec_db1': _L0_rec_in['db1'], 'L0_rec_dW2': _L0_rec_in['dW2'], 'L0_rec_db2': _L0_rec_in['db2'], 'L0_rec_dW3': _L0_rec_in['dW3'], 'L0_rec_db3': _L0_rec_in['db3'], 'L0_rec_Wo': _L0_rec_in['Wo'], 'L0_rec_bo': _L0_rec_in['bo']}

def reference(r_user, r_item, L0_rec_user_emb, L0_rec_item_emb, L0_rec_cw1, L0_rec_cw2, L0_rec_dW1, L0_rec_db1, L0_rec_dW2, L0_rec_db2, L0_rec_dW3, L0_rec_db3, L0_rec_Wo, L0_rec_bo):
    import jax
    import jax.numpy as jnp

    def _L0_rec_ref(user, item, user_emb, item_emb, cw1, cw2, dW1, db1, dW2, db2, dW3, db3, Wo, bo):
        import jax, jax.numpy as jnp
        import numpy as np
        B = 2048
        USER_NUM = 62500
        ITEM_NUM = 12500
        D = 512
        DEEP = [512, 256, 128, 64]
        ue = user_emb[user]
        ie = item_emb[item]
        x0 = jnp.concatenate([ue, ie], axis=-1)
        x1 = x0 * (x0 @ cw1)[:, None] + x0
        x2 = x0 * (x1 @ cw2)[:, None] + x1
        h = jax.nn.relu(x0 @ dW1 + db1)
        h = jax.nn.relu(h @ dW2 + db2)
        h = jax.nn.relu(h @ dW3 + db3)
        out = jnp.concatenate([x2, h], axis=-1) @ Wo + bo
        return out.reshape(-1)
    y = _L0_rec_ref(r_user, r_item, L0_rec_user_emb, L0_rec_item_emb, L0_rec_cw1, L0_rec_cw2, L0_rec_dW1, L0_rec_db1, L0_rec_dW2, L0_rec_db2, L0_rec_dW3, L0_rec_db3, L0_rec_Wo, L0_rec_bo)
    return y

_drawn_inputs = setup_inputs


def setup_inputs(seed=0):
    import zlib

    import numpy as np

    out = dict(_drawn_inputs(seed))
    spreads = {'L0_rec_db1': (0.0, 0.1), 'L0_rec_db2': (0.0, 0.1), 'L0_rec_db3': (0.0, 0.1)}
    factors = {'L0_rec_cw1': 27.056, 'L0_rec_cw2': 5.045, 'L0_rec_dW1': 8.0, 'L0_rec_dW2': 8.0}
    for name, (base, spread) in spreads.items():
        noise = np.random.default_rng([zlib.crc32(name.encode()), seed]).standard_normal(out[name].shape)
        drawn = base * np.exp(spread * noise) if base else spread * noise
        out[name] = jnp.asarray(drawn.astype(out[name].dtype))
    for name, factor in factors.items():
        out[name] = (out[name] * factor).astype(out[name].dtype)
    return out
```

```python
from contextlib import ExitStack

import concourse.bass as bass
from concourse import mybir

P = 128


def recommender(nc, user_ids, item_ids, user_emb, item_emb, cw1, cw2,
                dW1, db1, dW2, db2, dW3, db3, Wo, bo, scores):
    f32, f32r, i32 = mybir.dt.float32, mybir.dt.float32r, mybir.dt.int32
    ALU, ACT = mybir.AluOpType, mybir.ActivationFunctionType

    BATCH = user_ids.shape[0]
    HALF = user_emb.shape[1]
    D = 2 * HALF
    H1, H2, H3 = dW1.shape[1], dW2.shape[1], dW3.shape[1]
    TILES = BATCH // P
    S = 2
    N = S * P
    BLOCKS = TILES // S
    CH = HALF // P
    C1 = D // P
    C2 = H1 // P
    UNITS = 2 * BLOCKS
    TABLES = (user_emb, item_emb)
    DOTS = 3
    Q = 32

    with ExitStack() as ctx:
        def sb(name, shape, dt=f32):
            return ctx.enter_context(nc.sbuf_tensor(name, shape, dt))

        def psum(name):
            return ctx.enter_context(nc.psum_tensor(name, [P, 512], f32))

        def sem(name):
            return ctx.enter_context(nc.semaphore(name))

        ids = sb("ids", [P, 2, TILES], i32)
        rows_of = sb("rows_of", [P, 2, TILES])
        last_of = sb("last_of", [P, 2, TILES])
        wrap = sb("wrap", [P, 2, TILES])
        wrapped = sb("wrapped", [P, 2, TILES])
        row_ids = sb("row_ids", [P, 2, TILES], i32)
        x = sb("x", [P, UNITS, S, HALF])
        xT = sb("xT", [P, UNITS, CH, N])
        xT_hi = sb("xT_hi", [P, UNITS, CH, N], f32r)
        xT_lo = sb("xT_lo", [P, UNITS, CH, N], f32r)
        w1 = sb("w1", [P, C1, H1])
        w1_hi = sb("w1_hi", [P, C1, H1], f32r)
        w1_lo = sb("w1_lo", [P, C1, H1], f32r)
        w2 = sb("w2", [P, C2, H2])
        w2_hi = sb("w2_hi", [P, C2, H2], f32r)
        w2_lo = sb("w2_lo", [P, C2, H2], f32r)
        w3 = sb("w3", [P, H3])
        R_DOT, R_B1, R_B2, R_B3, R_WOH = 0, DOTS * C1, DOTS * C1 + C2, DOTS * C1 + C2 + 1, DOTS * C1 + C2 + 2
        ROWS = R_WOH + 1
        vec_rows = sb("vec_rows", [ROWS, P])
        vec = sb("vec", [P, ROWS])
        neg_b1 = sb("neg_b1", [P, C2])
        b2_folded = sb("b2_folded", [P, 1])
        bo_all = sb("bo_all", [P, 1])
        dot_w = sb("dot_w", [P, C1, Q])
        woh = sb("woh", [P, Q])
        ident = sb("ident", [P, P])
        h1_hi = sb("h1_hi", [P, 2, C2, N], f32r)
        h1_lo = sb("h1_lo", [P, 2, C2, N], f32r)
        h2 = sb("h2", [P, 2, N])
        h3 = sb("h3", [P, 2, N])
        dots = sb("dots", [P, 2, P])
        parts = sb("parts", [P, BLOCKS, S, 2, 4])
        both = sb("both", [P, TILES, 4])
        cross2 = sb("cross2", [P, TILES])
        cross = sb("cross", [P, TILES])
        score = sb("score", [P, TILES])

        tp = [psum("tp0"), psum("tp1")]
        h1p = [psum("h1p0"), psum("h1p1")]
        h2p, h3p, dotp, dotTp = psum("h2p"), psum("h3p"), psum("dotp"), psum("dotTp")

        ids_landed, vec_landed, w1_landed = sem("ids_landed"), sem("vec_landed"), sem("w1_landed")
        w2_landed, w3_landed, bo_landed = sem("w2_landed"), sem("w3_landed"), sem("bo_landed")
        x_landed = [sem(f"x_landed{k}") for k in range(UNITS)]
        limits_set, wrap_done, ids_ready = sem("limits_set"), sem("wrap_done"), sem("ids_ready")
        zeroed, ident_zeroed, ident_ready = sem("zeroed"), sem("ident_zeroed"), sem("ident_ready")
        vecT_done, vec_ready, cols_ready = sem("vecT_done"), sem("vec_ready"), sem("cols_ready")
        fold_done, b2_ready = sem("fold_done"), sem("b2_ready")
        w1_hi_ready, w1_lo_ready = sem("w1_hi_ready"), sem("w1_lo_ready")
        w2_hi_ready, w2_lo_ready = sem("w2_hi_ready"), sem("w2_lo_ready")
        xT_done, hi_ready, whole_ready, lo_ready = sem("xT_done"), sem("hi_ready"), sem("whole_ready"), sem("lo_ready")
        h1_done, h1_hi_ready, h1_lo_ready = sem("h1_done"), sem("h1_hi_ready"), sem("h1_lo_ready")
        h2_done, h2_ready, h3_done = sem("h2_done"), sem("h2_ready"), sem("h3_done")
        h3a_ready, h3b_ready = sem("h3a_ready"), sem("h3b_ready")
        dots_done, dots_ready, dotsT_done, parts_ready = sem("dots_done"), sem("dots_ready"), sem("dotsT_done"), sem("parts_ready")
        both_ready, cross2_ready, cross_ready, score_ready = sem("both_ready"), sem("cross2_ready"), sem("cross_ready"), sem("score_ready")
        stored = sem("stored")

        block = ctx.enter_context(nc.Block())

        @block.sync
        def _(sp):
            sp.dma_start(ids[:, 0, :], user_ids.rearrange("(p t) -> p t", t=TILES)).then_inc(ids_landed, 16)
            sp.dma_start(ids[:, 1, :], item_ids.rearrange("(p t) -> p t", t=TILES)).then_inc(ids_landed, 16)
            sp.dma_start(w1[:, :, :], dW1.rearrange("(c p) n -> p c n", p=P)).then_inc(w1_landed, 16)
            sp.dma_start(w2[:, :, :], dW2.rearrange("(c p) n -> p c n", p=P)).then_inc(w2_landed, 16)
            sp.dma_start(w3[:, :], dW3).then_inc(w3_landed, 16)
            sp.dma_start(bo_all[:, :], bo.rearrange("(a n) -> a n", a=1).to_broadcast([P, 1])).then_inc(bo_landed, 16)
            sp.wait_ge(score_ready, 1)
            sp.dma_start(scores.rearrange("(p t) -> p t", t=TILES), score[:, :]).then_inc(stored, 16)
            sp.wait_ge(stored, 16)

        @block.gpsimd
        def _(pool):
            pool.memset(ident[:, :], 0.0).then_inc(ident_zeroed, 1)
            pool.wait_ge(ident_zeroed, 1)
            pool.affine_select(out=ident[:, :], in_=ident[:, :], compare_op=ALU.not_equal, fill=1.0,
                               base=0, pattern=[[-1, P]], channel_multiplier=1).then_inc(ident_ready, 1)
            pool.wait_ge(ids_ready, 1)
            for k in range(UNITS):
                for s in range(S):
                    t = (k // 2) * S + s
                    pool.indirect_dma_start(
                        out=x[:, k, s, :], out_offset=None, in_=TABLES[k % 2],
                        in_offset=bass.IndirectOffsetOnAxis(ap=row_ids[:, k % 2, t:t + 1], axis=0),
                    ).then_inc(x_landed[k], 16)

        @block.scalar
        def _(act):
            row = lambda v, n: v.rearrange("(r n) -> r n", n=n)
            act.dma_start(vec_rows[R_DOT:R_DOT + C1, :], row(cw1, P)).then_inc(vec_landed, 16)
            act.dma_start(vec_rows[R_DOT + C1:R_DOT + 2 * C1, :], row(cw2, P)).then_inc(vec_landed, 16)
            act.dma_start(vec_rows[R_DOT + 2 * C1:R_B1, :], Wo[0:D, :].rearrange("(r n) o -> r (n o)", n=P)).then_inc(vec_landed, 16)
            act.dma_start(vec_rows[R_B1:R_B2, :], row(db1, P)).then_inc(vec_landed, 16)
            act.dma_start(vec_rows[R_B2:R_B3, :], row(db2, P)).then_inc(vec_landed, 16)
            for half in range(P // H3):
                cols = slice(half * H3, (half + 1) * H3)
                act.dma_start(vec_rows[R_B3:R_WOH, cols], row(db3, H3)).then_inc(vec_landed, 16)
                act.dma_start(vec_rows[R_WOH:ROWS, cols], Wo[D:D + H3, :].rearrange("(r n) o -> r (n o)", n=H3)).then_inc(vec_landed, 16)
            act.wait_ge(w1_landed, 16)
            nc.scalar.activation(w1_hi[:, :, :], w1[:, :, :], ACT.Copy).then_inc(w1_hi_ready, 1)
            act.wait_ge(w2_landed, 16)
            nc.scalar.activation(w2_hi[:, :, :], w2[:, :, :], ACT.Copy).then_inc(w2_hi_ready, 1)

            def split_units(k):
                for u in (k, k + 1):
                    act.wait_ge(xT_done, u + 1)
                    nc.scalar.activation(xT_hi[:, u, :, :], tp[u % 2][:, :], ACT.Copy).then_inc(hi_ready, 1)
                for u in (k, k + 1):
                    act.wait_ge(lo_ready, u + 1)
                    nc.scalar.activation(xT[:, u, :, :], tp[u % 2][:, :], ACT.Copy).then_inc(whole_ready, 1)

            split_units(0)
            for b in range(BLOCKS):
                if b >= 1:
                    act.wait_ge(dots_done, b)
                    if b >= 3:
                        act.wait_ge(dotsT_done, b - 2)
                    nc.scalar.activation(dots[:, (b - 1) % 2, :], dotp[:, 0:P], ACT.Copy).then_inc(dots_ready, 1)
                if b + 1 < BLOCKS:
                    split_units(2 * b + 2)
                act.wait_ge(h2_done, b + 1)
                if b == 0:
                    act.wait_ge(b2_ready, 1)
                if b >= 2:
                    act.wait_ge(h3_done, b - 1)
                nc.scalar.activation(h2[:, b % 2, :], h2p[:, 0:N], ACT.Relu, bias=b2_folded[:, 0:1]).then_inc(h2_ready, 1)
                act.wait_ge(h3_done, b + 1)
                if b >= 2:
                    act.wait_ge(dots_done, b - 1)
                if b == 0:
                    act.wait_ge(zeroed, 4)
                nc.scalar.activation(h3[0:H3, b % 2, 0:P], h3p[0:H3, 0:P], ACT.Relu,
                                     bias=vec[0:H3, R_B3:R_B3 + 1]).then_inc(h3a_ready, 1)
            act.wait_ge(dots_done, BLOCKS)
            act.wait_ge(dotsT_done, BLOCKS - 2)
            nc.scalar.activation(dots[:, (BLOCKS - 1) % 2, :], dotp[:, 0:P], ACT.Copy).then_inc(dots_ready, 1)

        @block.vector
        def _(dve):
            for table in range(2):
                nc.vector.memset(rows_of[:, table, :], float(TABLES[table].shape[0])).then_inc(limits_set, 1)
                nc.vector.memset(last_of[:, table, :], float(TABLES[table].shape[0] - 1)).then_inc(limits_set, 1)
            nc.vector.memset(dot_w[:, :, :], 0.0).then_inc(zeroed, 1)
            nc.vector.memset(woh[:, :], 0.0).then_inc(zeroed, 1)
            for buf in range(2):
                nc.vector.memset(h3[H3:P, buf, :], 0.0).then_inc(zeroed, 1)
            dve.wait_ge(limits_set, 4)
            dve.wait_ge(ids_landed, 32)
            nc.vector.scalar_tensor_tensor(wrap[:, :, :], ids[:, :, :], 0.0, rows_of[:, :, :],
                                           ALU.is_lt, ALU.mult).then_inc(wrap_done, 1)
            dve.wait_ge(wrap_done, 1)
            nc.vector.tensor_tensor(wrapped[:, :, :], wrap[:, :, :], ids[:, :, :], ALU.add).then_inc(wrap_done, 1)
            dve.wait_ge(wrap_done, 2)
            nc.vector.scalar_tensor_tensor(row_ids[:, :, :], wrapped[:, :, :], 0.0, last_of[:, :, :],
                                           ALU.max, ALU.min).then_inc(ids_ready, 1)
            dve.wait_ge(w1_hi_ready, 1)
            nc.vector.tensor_tensor(w1_lo[:, :, :], w1[:, :, :], w1_hi[:, :, :].bitcast(f32), ALU.subtract).then_inc(w1_lo_ready, 1)
            dve.wait_ge(w2_hi_ready, 1)
            nc.vector.tensor_tensor(w2_lo[:, :, :], w2[:, :, :], w2_hi[:, :, :].bitcast(f32), ALU.subtract).then_inc(w2_lo_ready, 1)
            dve.wait_ge(vecT_done, 1)
            nc.vector.tensor_copy(vec[:, :], h2p[:, 0:ROWS]).then_inc(vec_ready, 1)
            dve.wait_ge(vec_ready, 1)
            dve.wait_ge(zeroed, 4)
            nc.vector.tensor_copy(dot_w[:, :, 0:DOTS],
                                  vec[:, R_DOT:R_B1].rearrange("p (i c) -> p c i", c=C1)).then_inc(cols_ready, 1)
            nc.vector.tensor_copy(woh[0:H3, DOTS:DOTS + 1], vec[0:H3, R_WOH:ROWS]).then_inc(cols_ready, 1)
            nc.vector.tensor_scalar(neg_b1[:, :], vec[:, R_B1:R_B2], -1.0, None, ALU.mult).then_inc(cols_ready, 1)
            dve.wait_ge(fold_done, 1)
            nc.vector.tensor_tensor(b2_folded[:, :], h3p[:, 0:1], vec[:, R_B2:R_B3], ALU.add).then_inc(b2_ready, 1)
            dve.wait_ge(cols_ready, 3)

            def split_unit(k):
                dve.wait_ge(hi_ready, k + 1)
                nc.vector.tensor_tensor(xT_lo[:, k, :, :], tp[k % 2][:, :].rearrange("p (c n) -> p c n", c=CH),
                                        xT_hi[:, k, :, :].bitcast(f32), ALU.subtract).then_inc(lo_ready, 1)

            def part_of_scores(b):
                dve.wait_ge(dotsT_done, b + 1)
                nc.vector.tensor_copy(parts[:, b, :, :, :],
                                      dotTp[:, 0:P].rearrange("p (s h q) -> p s h q", s=S, h=2)[:, :, :, 0:4]).then_inc(parts_ready, 1)

            split_unit(0)
            split_unit(1)
            for b in range(BLOCKS):
                for n in range(C2):
                    dve.wait_ge(h1_done, C2 * b + n + 1)
                    if b >= 2:
                        dve.wait_ge(h2_done, b - 1)
                    nc.vector.tensor_scalar(h1_hi[:, b % 2, n, :], h1p[n][:, 0:N], neg_b1[:, n:n + 1], None,
                                            ALU.max).then_inc(h1_hi_ready, 1)
                    dve.wait_ge(h1_hi_ready, C2 * b + n + 1)
                    nc.vector.scalar_tensor_tensor(h1_lo[:, b % 2, n, :], h1p[n][:, 0:N], neg_b1[:, n:n + 1],
                                                   h1_hi[:, b % 2, n, :].bitcast(f32),
                                                   ALU.max, ALU.subtract).then_inc(h1_lo_ready, 1)
                if b >= 1:
                    part_of_scores(b - 1)
                if b + 1 < BLOCKS:
                    split_unit(2 * b + 2)
                    split_unit(2 * b + 3)
                dve.wait_ge(h3_done, b + 1)
                if b >= 2:
                    dve.wait_ge(dots_done, b - 1)
                nc.vector.tensor_scalar(h3[0:H3, b % 2, P:N], h3p[H3:P, 0:P], vec[H3:P, R_B3:R_B3 + 1], 0.0,
                                        ALU.add, ALU.max).then_inc(h3b_ready, 1)
            part_of_scores(BLOCKS - 1)
            dve.wait_ge(parts_ready, BLOCKS)
            of_tile = parts[:, :, :, :, :].rearrange("p b s h i -> p (b s) h i")
            nc.vector.tensor_tensor(both[:, :, :], of_tile[:, :, 0, :], of_tile[:, :, 1, :], ALU.add).then_inc(both_ready, 1)
            dve.wait_ge(both_ready, 1)
            nc.vector.scalar_tensor_tensor(cross2[:, :], both[:, :, 1], 1.0, both[:, :, 2], ALU.add, ALU.mult).then_inc(cross2_ready, 1)
            dve.wait_ge(cross2_ready, 1)
            nc.vector.scalar_tensor_tensor(cross[:, :], both[:, :, 0], 1.0, cross2[:, :], ALU.add, ALU.mult).then_inc(cross_ready, 1)
            dve.wait_ge(cross_ready, 1)
            dve.wait_ge(bo_landed, 16)
            nc.vector.scalar_tensor_tensor(score[:, :], both[:, :, 3], bo_all[:, 0:1], cross[:, :], ALU.add, ALU.add).then_inc(score_ready, 1)

        @block.tensor
        def _(pe):
            mm = nc.tensor.matmul
            pe.wait_ge(ident_ready, 1)
            pe.wait_ge(vec_landed, 16 * (5 + 2 * (P // H3)))
            nc.tensor.transpose(h2p[:, 0:ROWS], vec_rows[:, :], ident[0:ROWS, 0:ROWS]).then_inc(vecT_done, 1)
            pe.wait_ge(vec_ready, 1)
            pe.wait_ge(w2_landed, 16)
            for c in range(C2):
                last = mm(h3p[:, 0:1], w2[:, c, :], vec[:, R_B1 + c:R_B1 + c + 1], start=(c == 0), stop=(c == C2 - 1))
            last.then_inc(fold_done, 1)

            def transpose_unit(k):
                pe.wait_ge(x_landed[k], 16 * S)
                if k >= 2:
                    pe.wait_ge(whole_ready, k - 1)
                for s in range(S):
                    for c in range(CH):
                        last = nc.tensor.transpose(tp[k % 2][:, c * N + s * P:c * N + (s + 1) * P],
                                                   x[:, k, s, c * P:(c + 1) * P], ident[:, :])
                last.then_inc(xT_done, 1)

            def layer1_half(b, table):
                k = 2 * b + table
                pe.wait_ge(hi_ready, k + 1)
                pe.wait_ge(lo_ready, k + 1)
                for n in range(C2):
                    if table == 0 and b >= 1:
                        pe.wait_ge(h1_lo_ready, C2 * (b - 1) + n + 1)
                    cols = slice(n * P, (n + 1) * P)
                    for c in range(CH):
                        wc = table * CH + c
                        mm(h1p[n][:, 0:N], w1_hi[:, wc, cols], xT_hi[:, k, c, :], start=(wc == 0), stop=False)
                        mm(h1p[n][:, 0:N], w1_hi[:, wc, cols], xT_lo[:, k, c, :], start=False, stop=False)
                        last = mm(h1p[n][:, 0:N], w1_lo[:, wc, cols], xT_hi[:, k, c, :], start=False, stop=(wc == C1 - 1))
                    if table == 1:
                        last.then_inc(h1_done, 1)

            def layer2(b):
                if b == 0:
                    pe.wait_ge(w2_lo_ready, 1)
                else:
                    pe.wait_ge(h2_ready, b)
                for c in range(C2):
                    pe.wait_ge(h1_lo_ready, C2 * b + c + 1)
                    mm(h2p[:, 0:N], w2_hi[:, c, :], h1_hi[:, b % 2, c, :], start=(c == 0), stop=False)
                    mm(h2p[:, 0:N], w2_hi[:, c, :], h1_lo[:, b % 2, c, :], start=False, stop=False)
                    last = mm(h2p[:, 0:N], w2_lo[:, c, :], h1_hi[:, b % 2, c, :], start=False, stop=(c == C2 - 1))
                last.then_inc(h2_done, 1)

            def dot_products(b):
                if b == 0:
                    pe.wait_ge(cols_ready, 3)
                else:
                    pe.wait_ge(dots_ready, b)
                pe.wait_ge(whole_ready, 2 * b + 2)
                for c in range(CH):
                    for s in range(S):
                        for table in range(2):
                            q = Q * (2 * s + table)
                            mm(dotp[q:q + Q, 0:P], dot_w[:, table * CH + c, :],
                               xT[:, 2 * b + table, c, s * P:(s + 1) * P],
                               start=(c == 0), stop=(c == CH - 1 and table == 1))

            def layer3(b):
                if b == 0:
                    pe.wait_ge(w3_landed, 16)
                    pe.wait_ge(b2_ready, 1)
                else:
                    pe.wait_ge(h3a_ready, b)
                    pe.wait_ge(h3b_ready, b)
                pe.wait_ge(h2_ready, b + 1)
                for s in range(S):
                    last = mm(h3p[s * H3:(s + 1) * H3, 0:P], w3[:, :], h2[:, b % 2, s * P:(s + 1) * P], start=True, stop=True)
                last.then_inc(h3_done, 1)

            def last_dot(b):
                pe.wait_ge(h3a_ready, b + 1)
                pe.wait_ge(h3b_ready, b + 1)
                for s in range(S):
                    q = Q * 2 * s
                    last = mm(dotp[q:q + Q, 0:P], woh[:, :], h3[:, b % 2, s * P:(s + 1) * P], start=False, stop=True)
                last.then_inc(dots_done, 1)

            def dots_to_rows(b):
                pe.wait_ge(dots_ready, b + 1)
                if b >= 1:
                    pe.wait_ge(parts_ready, b)
                nc.tensor.transpose(dotTp[:, 0:P], dots[:, b % 2, :], ident[:, :]).then_inc(dotsT_done, 1)

            transpose_unit(0)
            pe.wait_ge(w1_lo_ready, 1)
            for b in range(BLOCKS):
                layer1_half(b, 0)
                if b == 0:
                    transpose_unit(1)
                else:
                    last_dot(b - 1)
                layer1_half(b, 1)
                if b >= 1:
                    dots_to_rows(b - 1)
                if b + 1 < BLOCKS:
                    transpose_unit(2 * b + 2)
                    transpose_unit(2 * b + 3)
                layer2(b)
                dot_products(b)
                layer3(b)
            last_dot(BLOCKS - 1)
            dots_to_rows(BLOCKS - 1)


INPUTS = ["r_user", "r_item", "L0_rec_user_emb", "L0_rec_item_emb", "L0_rec_cw1", "L0_rec_cw2",
          "L0_rec_dW1", "L0_rec_db1", "L0_rec_dW2", "L0_rec_db2", "L0_rec_dW3", "L0_rec_db3",
          "L0_rec_Wo", "L0_rec_bo"]


def kernel(**inputs):
    import numpy as np
    import concourse.bacc as bacc
    from concourse.bass_utils import run_bass_kernel_spmd

    nc = bacc.Bacc("TRN2", target_bir_lowering=False, num_devices=1)
    arrays = {name: np.ascontiguousarray(inputs[name]) for name in INPUTS}
    args = [nc.dram_tensor(name, a.shape, mybir.dt.from_np(a.dtype), kind="ExternalInput").ap()
            for name, a in arrays.items()]
    batch = arrays["r_user"].shape[0]
    scores = nc.dram_tensor("scores", (batch,), mybir.dt.float32, kind="ExternalOutput").ap()
    recommender(nc, *args, scores)
    ran = run_bass_kernel_spmd(nc, [arrays], core_ids=[0])
    return ran.results[0]["scores"]
```

```python
from contextlib import ExitStack

import concourse.bass as bass
from concourse import mybir

P = 128


def recommender(nc, user_ids, item_ids, user_emb, item_emb, cw1, cw2,
                dW1, db1, dW2, db2, dW3, db3, Wo, bo, scores):
    f32, f32r, i32 = mybir.dt.float32, mybir.dt.float32r, mybir.dt.int32
    ALU, ACT = mybir.AluOpType, mybir.ActivationFunctionType

    BATCH = user_ids.shape[0]
    HALF = user_emb.shape[1]
    D = 2 * HALF
    H1, H2, H3 = dW1.shape[1], dW2.shape[1], dW3.shape[1]
    TILES = BATCH // P
    S = 2
    N = S * P
    BLOCKS = TILES // S
    CH = HALF // P
    C1 = D // P
    C2 = H1 // P
    UNITS = 2 * BLOCKS
    TABLES = (user_emb, item_emb)
    DOTS = 3
    WARM_UP = 16
    Q = 32

    with ExitStack() as ctx:
        def sb(name, shape, dt=f32):
            return ctx.enter_context(nc.sbuf_tensor(name, shape, dt))

        def psum(name):
            return ctx.enter_context(nc.psum_tensor(name, [P, 512], f32))

        def sem(name):
            return ctx.enter_context(nc.semaphore(name))

        ids = sb("ids", [P, 2, TILES], i32)
        rows_of = sb("rows_of", [P, 2, TILES])
        last_of = sb("last_of", [P, 2, TILES])
        wrap = sb("wrap", [P, 2, TILES])
        wrapped = sb("wrapped", [P, 2, TILES])
        row_ids = sb("row_ids", [P, 2, TILES], i32)
        x = sb("x", [P, UNITS, S, HALF])
        xT = sb("xT", [P, UNITS, CH, N])
        xT_hi = sb("xT_hi", [P, UNITS, CH, N], f32r)
        xT_lo = sb("xT_lo", [P, UNITS, CH, N], f32r)
        w1 = sb("w1", [P, C1, H1])
        w1_hi = sb("w1_hi", [P, C1, H1], f32r)
        w1_lo = sb("w1_lo", [P, C1, H1], f32r)
        w2 = sb("w2", [P, C2, H2])
        w2_hi = sb("w2_hi", [P, C2, H2], f32r)
        w2_lo = sb("w2_lo", [P, C2, H2], f32r)
        w3 = sb("w3", [P, H3])
        R_DOT, R_B1, R_B2, R_B3, R_WOH = 0, DOTS * C1, DOTS * C1 + C2, DOTS * C1 + C2 + 1, DOTS * C1 + C2 + 2
        ROWS = R_WOH + 1
        vec_rows = sb("vec_rows", [ROWS, P])
        vec = sb("vec", [P, ROWS])
        neg_b1 = sb("neg_b1", [P, C2])
        b2_folded = sb("b2_folded", [P, 1])
        bo_all = sb("bo_all", [P, 1])
        dot_w = sb("dot_w", [P, C1, Q])
        woh = sb("woh", [P, Q])
        ident = sb("ident", [P, P])
        h1_hi = sb("h1_hi", [P, 2, C2, N], f32r)
        h1_lo = sb("h1_lo", [P, 2, C2, N], f32r)
        h2 = sb("h2", [P, 2, N])
        h3 = sb("h3", [P, 2, N])
        dots = sb("dots", [P, 2, P])
        parts = sb("parts", [P, BLOCKS, S, 2, 4])
        both = sb("both", [P, TILES, 4])
        cross2 = sb("cross2", [P, TILES])
        cross = sb("cross", [P, TILES])
        score = sb("score", [P, TILES])

        tp = [psum("tp0"), psum("tp1")]
        h1p = [[psum(f"h1p{buf}{n}") for n in range(C2)] for buf in range(2)]
        h23_bank, dot_bank = psum("h23_bank"), psum("dot_bank")
        h2p, h3p = h23_bank[:, 0:N], h23_bank[:, N:N + P]
        dotp, dotTp = dot_bank[:, 0:P], dot_bank[:, P:2 * P]

        ids_landed, vec_landed, w1_landed = sem("ids_landed"), sem("vec_landed"), sem("w1_landed")
        w2_landed, w3_landed, bo_landed = sem("w2_landed"), sem("w3_landed"), sem("bo_landed")
        x_landed = [sem(f"x_landed{k}") for k in range(UNITS)]
        limits_set, wrap_done, ids_ready = sem("limits_set"), sem("wrap_done"), sem("ids_ready")
        zeroed, ident_zeroed, ident_ready = sem("zeroed"), sem("ident_zeroed"), sem("ident_ready")
        vecT_done, vec_ready, cols_ready = sem("vecT_done"), sem("vec_ready"), sem("cols_ready")
        fold_done, b2_ready = sem("fold_done"), sem("b2_ready")
        w1_hi_ready, w1_lo_ready = sem("w1_hi_ready"), sem("w1_lo_ready")
        w2_hi_ready, w2_lo_ready = sem("w2_hi_ready"), sem("w2_lo_ready")
        xT_done, hi_ready, whole_ready, lo_ready = sem("xT_done"), sem("hi_ready"), sem("whole_ready"), sem("lo_ready")
        h1_done, h1_hi_ready, h1_lo_ready = sem("h1_done"), sem("h1_hi_ready"), sem("h1_lo_ready")
        h2_done, h2_ready, h3_done = sem("h2_done"), sem("h2_ready"), sem("h3_done")
        h3a_ready, h3b_ready = sem("h3a_ready"), sem("h3b_ready")
        dots_done, dots_ready, dotsT_done, parts_ready = sem("dots_done"), sem("dots_ready"), sem("dotsT_done"), sem("parts_ready")
        both_ready, cross2_ready, cross_ready, score_ready = sem("both_ready"), sem("cross2_ready"), sem("cross_ready"), sem("score_ready")
        stored = sem("stored")

        block = ctx.enter_context(nc.Block())

        @block.sync
        def _(sp):
            sp.dma_start(ids[:, 0, :], user_ids.rearrange("(p t) -> p t", t=TILES)).then_inc(ids_landed, 16)
            sp.dma_start(ids[:, 1, :], item_ids.rearrange("(p t) -> p t", t=TILES)).then_inc(ids_landed, 16)
            sp.dma_start(w1[:, :, :], dW1.rearrange("(c p) n -> p c n", p=P)).then_inc(w1_landed, 16)
            row = lambda v, n: v.rearrange("(r n) -> r n", n=n)
            twice = lambda v: v.rearrange("(a r n) -> a r n", a=1, r=1).to_broadcast([1, P // H3, H3])
            sp.dma_start(vec_rows[R_B1:R_B2, :], row(db1, P)).then_inc(vec_landed, 16)
            sp.dma_start(vec_rows[R_B2:R_B3, :], row(db2, P)).then_inc(vec_landed, 16)
            sp.dma_start(w2[:, :, :], dW2.rearrange("(c p) n -> p c n", p=P)).then_inc(w2_landed, 16)
            sp.dma_start(vec_rows[R_DOT:R_DOT + C1, :], row(cw1, P)).then_inc(vec_landed, 16)
            sp.dma_start(vec_rows[R_DOT + C1:R_DOT + 2 * C1, :], row(cw2, P)).then_inc(vec_landed, 16)
            sp.dma_start(vec_rows[R_DOT + 2 * C1:R_B1, :], Wo[0:D, :].rearrange("(r n) o -> r (n o)", n=P)).then_inc(vec_landed, 16)
            sp.dma_start(vec_rows[R_B3:R_WOH, :].rearrange("a (r n) -> a r n", n=H3), twice(db3)).then_inc(vec_landed, 16)
            sp.dma_start(vec_rows[R_WOH:ROWS, :].rearrange("a (r n) -> a r n", n=H3),
                         twice(Wo[D:D + H3, :].rearrange("n o -> (n o)"))).then_inc(vec_landed, 16)
            sp.dma_start(w3[:, :], dW3).then_inc(w3_landed, 16)
            sp.dma_start(bo_all[:, :], bo.rearrange("(a n) -> a n", a=1).to_broadcast([P, 1])).then_inc(bo_landed, 16)
            sp.wait_ge(score_ready, 1)
            sp.dma_start(scores.rearrange("(p t) -> p t", t=TILES), score[:, :]).then_inc(stored, 16)
            sp.wait_ge(stored, 16)

        @block.gpsimd
        def _(pool):
            pool.memset(ident[:, :], 0.0).then_inc(ident_zeroed, 1)
            pool.wait_ge(ident_zeroed, 1)
            pool.affine_select(out=ident[:, :], in_=ident[:, :], compare_op=ALU.not_equal, fill=1.0,
                               base=0, pattern=[[-1, P]], channel_multiplier=1).then_inc(ident_ready, 1)
            pool.wait_ge(ids_ready, 1)
            for k in range(UNITS):
                for s in range(S):
                    t = (k // 2) * S + s
                    pool.indirect_dma_start(
                        out=x[:, k, s, :], out_offset=None, in_=TABLES[k % 2],
                        in_offset=bass.IndirectOffsetOnAxis(ap=row_ids[:, k % 2, t:t + 1], axis=0),
                    ).then_inc(x_landed[k], 16)

        @block.scalar
        def _(act):
            act.preload_act_table(ACT.Relu)
            act.wait_ge(w1_landed, 16)
            nc.scalar.activation(w1_hi[:, :, :], w1[:, :, :], ACT.Copy).then_inc(w1_hi_ready, 1)
            act.wait_ge(w2_landed, 16)
            nc.scalar.activation(w2_hi[:, :, :], w2[:, :, :], ACT.Copy).then_inc(w2_hi_ready, 1)

            def hi_of(k):
                act.wait_ge(xT_done, k + 1)
                nc.scalar.activation(xT_hi[:, k, :, :], tp[k % 2][:, :], ACT.Copy).then_inc(hi_ready, 1)

            def whole_of(k):
                act.wait_ge(lo_ready, k + 1)
                nc.scalar.activation(xT[:, k, :, :], tp[k % 2][:, :], ACT.Copy).then_inc(whole_ready, 1)

            def keep_h2(b):
                act.wait_ge(h2_done, b + 1)
                if b == 0:
                    act.wait_ge(b2_ready, 1)
                if b >= 2:
                    act.wait_ge(h3_done, b - 1)
                nc.scalar.activation(h2[:, b % 2, :], h2p[:, 0:N], ACT.Relu, bias=b2_folded[:, 0:1]).then_inc(h2_ready, 1)

            def keep_h3_first(b):
                act.wait_ge(h3_done, b + 1)
                if b == 0:
                    act.wait_ge(zeroed, 4)
                if b >= 2:
                    act.wait_ge(dots_done, b - 1)
                nc.scalar.activation(h3[0:H3, b % 2, 0:P], h3p[0:H3, 0:P], ACT.Relu,
                                     bias=vec[0:H3, R_B3:R_B3 + 1]).then_inc(h3a_ready, 1)

            def keep_dots(b):
                act.wait_ge(dots_done, b + 1)
                if b >= 2:
                    act.wait_ge(dotsT_done, b - 1)
                nc.scalar.activation(dots[:, b % 2, :], dotp[:, 0:P], ACT.Copy).then_inc(dots_ready, 1)

            hi_of(0)
            whole_of(0)
            for b in range(BLOCKS):
                if b >= 2:
                    keep_dots(b - 2)
                hi_of(2 * b + 1)
                if b >= 1:
                    keep_h2(b - 1)
                whole_of(2 * b + 1)
                if b + 1 < BLOCKS:
                    hi_of(2 * b + 2)
                if b >= 1:
                    keep_h3_first(b - 1)
                if b + 1 < BLOCKS:
                    whole_of(2 * b + 2)
            keep_dots(BLOCKS - 2)
            keep_h2(BLOCKS - 1)
            keep_h3_first(BLOCKS - 1)
            keep_dots(BLOCKS - 1)

        @block.vector
        def _(dve):
            for table in range(2):
                nc.vector.memset(rows_of[:, table, :], float(TABLES[table].shape[0])).then_inc(limits_set, 1)
                nc.vector.memset(last_of[:, table, :], float(TABLES[table].shape[0] - 1)).then_inc(limits_set, 1)
            nc.vector.memset(dot_w[:, :, :], 0.0).then_inc(zeroed, 1)
            nc.vector.memset(woh[:, :], 0.0).then_inc(zeroed, 1)
            for buf in range(2):
                nc.vector.memset(h3[H3:P, buf, :], 0.0).then_inc(zeroed, 1)
            dve.wait_ge(limits_set, 4)
            dve.wait_ge(ids_landed, 32)
            nc.vector.scalar_tensor_tensor(wrap[:, :, :], ids[:, :, :], 0.0, rows_of[:, :, :],
                                           ALU.is_lt, ALU.mult).then_inc(wrap_done, 1)
            dve.wait_ge(wrap_done, 1)
            nc.vector.tensor_tensor(wrapped[:, :, :], wrap[:, :, :], ids[:, :, :], ALU.add).then_inc(wrap_done, 1)
            dve.wait_ge(wrap_done, 2)
            nc.vector.scalar_tensor_tensor(row_ids[:, :, :], wrapped[:, :, :], 0.0, last_of[:, :, :],
                                           ALU.max, ALU.min).then_inc(ids_ready, 1)
            def lo_of(k):
                dve.wait_ge(hi_ready, k + 1)
                nc.vector.tensor_tensor(xT_lo[:, k, :, :], tp[k % 2][:, :].rearrange("p (c n) -> p c n", c=CH),
                                        xT_hi[:, k, :, :].bitcast(f32), ALU.subtract).then_inc(lo_ready, 1)

            dve.wait_ge(w1_hi_ready, 1)
            nc.vector.tensor_tensor(w1_lo[:, :, :], w1[:, :, :], w1_hi[:, :, :].bitcast(f32), ALU.subtract).then_inc(w1_lo_ready, 1)
            dve.wait_ge(vecT_done, 1)
            nc.vector.tensor_copy(vec[:, :], h2p[:, 0:ROWS]).then_inc(vec_ready, 1)
            dve.wait_ge(vec_ready, 1)
            dve.wait_ge(zeroed, 4)
            nc.vector.tensor_copy(dot_w[:, :, 0:DOTS],
                                  vec[:, R_DOT:R_B1].rearrange("p (i c) -> p c i", c=C1)).then_inc(cols_ready, 1)
            nc.vector.tensor_copy(woh[0:H3, DOTS:DOTS + 1], vec[0:H3, R_WOH:ROWS]).then_inc(cols_ready, 1)
            nc.vector.tensor_scalar(neg_b1[:, :], vec[:, R_B1:R_B2], -1.0, None, ALU.mult).then_inc(cols_ready, 1)
            dve.wait_ge(fold_done, 1)
            nc.vector.tensor_tensor(b2_folded[:, :], h3p[:, 0:1], vec[:, R_B2:R_B3], ALU.add).then_inc(b2_ready, 1)
            dve.wait_ge(cols_ready, 3)

            lo_of(0)
            dve.wait_ge(w2_hi_ready, 1)
            nc.vector.tensor_tensor(w2_lo[:, :, :], w2[:, :, :], w2_hi[:, :, :].bitcast(f32), ALU.subtract).then_inc(w2_lo_ready, 1)
            def keep_h1(b):
                for n in range(C2):
                    dve.wait_ge(h1_done, C2 * b + n + 1)
                    if b >= 2:
                        dve.wait_ge(h2_done, b - 1)
                    nc.vector.tensor_scalar(h1_hi[:, b % 2, n, :], h1p[b % 2][n][:, 0:N], neg_b1[:, n:n + 1], None,
                                            ALU.max).then_inc(h1_hi_ready, 1)
                    dve.wait_ge(h1_hi_ready, C2 * b + n + 1)
                    nc.vector.scalar_tensor_tensor(h1_lo[:, b % 2, n, :], h1p[b % 2][n][:, 0:N], neg_b1[:, n:n + 1],
                                                   h1_hi[:, b % 2, n, :].bitcast(f32),
                                                   ALU.max, ALU.subtract).then_inc(h1_lo_ready, 1)

            def keep_h3_second(b):
                dve.wait_ge(h3_done, b + 1)
                if b >= 2:
                    dve.wait_ge(dots_done, b - 1)
                nc.vector.tensor_scalar(h3[0:H3, b % 2, P:N], h3p[H3:P, 0:P], vec[H3:P, R_B3:R_B3 + 1], 0.0,
                                        ALU.add, ALU.max).then_inc(h3b_ready, 1)

            def keep_parts(b):
                dve.wait_ge(dotsT_done, b + 1)
                nc.vector.tensor_copy(parts[:, b, :, :, :],
                                      dotTp[:, 0:P].rearrange("p (s h q) -> p s h q", s=S, h=2)[:, :, :, 0:4]).then_inc(parts_ready, 1)

            for b in range(BLOCKS):
                if b >= 2:
                    keep_parts(b - 2)
                lo_of(2 * b + 1)
                if b >= 1:
                    keep_h3_second(b - 1)
                if b + 1 < BLOCKS:
                    lo_of(2 * b + 2)
                keep_h1(b)
            keep_parts(BLOCKS - 2)
            keep_h3_second(BLOCKS - 1)
            keep_parts(BLOCKS - 1)
            dve.wait_ge(parts_ready, BLOCKS)
            of_tile = parts[:, :, :, :, :].rearrange("p b s h i -> p (b s) h i")
            nc.vector.tensor_tensor(both[:, :, :], of_tile[:, :, 0, :], of_tile[:, :, 1, :], ALU.add).then_inc(both_ready, 1)
            dve.wait_ge(both_ready, 1)
            nc.vector.scalar_tensor_tensor(cross2[:, :], both[:, :, 1], 1.0, both[:, :, 2], ALU.add, ALU.mult).then_inc(cross2_ready, 1)
            dve.wait_ge(cross2_ready, 1)
            nc.vector.scalar_tensor_tensor(cross[:, :], both[:, :, 0], 1.0, cross2[:, :], ALU.add, ALU.mult).then_inc(cross_ready, 1)
            dve.wait_ge(cross_ready, 1)
            dve.wait_ge(bo_landed, 16)
            nc.vector.scalar_tensor_tensor(score[:, :], both[:, :, 3], bo_all[:, 0:1], cross[:, :], ALU.add, ALU.add).then_inc(score_ready, 1)

        @block.tensor
        def _(pe):
            mm = nc.tensor.matmul
            def set_up_vectors():
                pe.wait_ge(vec_landed, 16 * 7)
                nc.tensor.transpose(h2p[:, 0:ROWS], vec_rows[:, :], ident[0:ROWS, 0:ROWS]).then_inc(vecT_done, 1)
                pe.wait_ge(vec_ready, 1)
                pe.wait_ge(w2_landed, 16)
                for c in range(C2):
                    last = mm(h3p[:, 0:1], w2[:, c, :], vec[:, R_B1 + c:R_B1 + c + 1], start=(c == 0), stop=(c == C2 - 1))
                last.then_inc(fold_done, 1)

            def transpose_unit(k):
                pe.wait_ge(x_landed[k], 16 * S)
                if k >= 2:
                    pe.wait_ge(whole_ready, k - 1)
                for s in range(S):
                    for c in range(CH):
                        last = nc.tensor.transpose(tp[k % 2][:, c * N + s * P:c * N + (s + 1) * P],
                                                   x[:, k, s, c * P:(c + 1) * P], ident[:, :])
                last.then_inc(xT_done, 1)

            def layer1_half(b, table):
                k = 2 * b + table
                pe.wait_ge(hi_ready, k + 1)
                pe.wait_ge(lo_ready, k + 1)
                for n in range(C2):
                    if table == 0 and b >= 2:
                        pe.wait_ge(h1_lo_ready, C2 * (b - 2) + n + 1)
                    cols = slice(n * P, (n + 1) * P)
                    for c in range(CH):
                        wc = table * CH + c
                        mm(h1p[b % 2][n][:, 0:N], w1_hi[:, wc, cols], xT_hi[:, k, c, :], start=(wc == 0), stop=False)
                        mm(h1p[b % 2][n][:, 0:N], w1_hi[:, wc, cols], xT_lo[:, k, c, :], start=False, stop=False)
                        last = mm(h1p[b % 2][n][:, 0:N], w1_lo[:, wc, cols], xT_hi[:, k, c, :], start=False, stop=(wc == C1 - 1))
                    if table == 1:
                        last.then_inc(h1_done, 1)

            def layer2(b):
                if b == 0:
                    pe.wait_ge(w2_lo_ready, 1)
                    pe.wait_ge(b2_ready, 1)
                else:
                    pe.wait_ge(h3a_ready, b)
                    pe.wait_ge(h3b_ready, b)
                for c in range(C2):
                    pe.wait_ge(h1_lo_ready, C2 * b + c + 1)
                    mm(h2p[:, 0:N], w2_hi[:, c, :], h1_hi[:, b % 2, c, :], start=(c == 0), stop=False)
                    mm(h2p[:, 0:N], w2_hi[:, c, :], h1_lo[:, b % 2, c, :], start=False, stop=False)
                    last = mm(h2p[:, 0:N], w2_lo[:, c, :], h1_hi[:, b % 2, c, :], start=False, stop=(c == C2 - 1))
                last.then_inc(h2_done, 1)

            def dot_products(b):
                if b == 0:
                    pe.wait_ge(cols_ready, 3)
                else:
                    pe.wait_ge(parts_ready, b)
                pe.wait_ge(whole_ready, 2 * b + 2)
                for c in range(CH):
                    for s in range(S):
                        for table in range(2):
                            q = Q * (2 * s + table)
                            mm(dotp[q:q + Q, 0:P], dot_w[:, table * CH + c, :],
                               xT[:, 2 * b + table, c, s * P:(s + 1) * P],
                               start=(c == 0), stop=(c == CH - 1 and table == 1))

            def layer3(b):
                if b == 0:
                    pe.wait_ge(w3_landed, 16)
                pe.wait_ge(h2_ready, b + 1)
                for s in range(S):
                    last = mm(h3p[s * H3:(s + 1) * H3, 0:P], w3[:, :], h2[:, b % 2, s * P:(s + 1) * P], start=True, stop=True)
                last.then_inc(h3_done, 1)

            def last_dot(b):
                pe.wait_ge(h3a_ready, b + 1)
                pe.wait_ge(h3b_ready, b + 1)
                for s in range(S):
                    q = Q * 2 * s
                    last = mm(dotp[q:q + Q, 0:P], woh[:, :], h3[:, b % 2, s * P:(s + 1) * P], start=False, stop=True)
                last.then_inc(dots_done, 1)

            def dots_to_rows(b):
                pe.wait_ge(dots_ready, b + 1)
                nc.tensor.transpose(dotTp[:, 0:P], dots[:, b % 2, :], ident[:, :]).then_inc(dotsT_done, 1)

            pe.wait_ge(ident_ready, 1)
            for _ in range(WARM_UP):
                mm(dotp, ident[:, :], ident[:, :], start=True, stop=True)
            transpose_unit(0)
            set_up_vectors()
            pe.wait_ge(w1_lo_ready, 1)
            for b in range(BLOCKS):
                layer1_half(b, 0)
                if b >= 2:
                    dots_to_rows(b - 2)
                transpose_unit(2 * b + 1)
                if b >= 1:
                    layer2(b - 1)
                    dot_products(b - 1)
                if b + 1 < BLOCKS:
                    transpose_unit(2 * b + 2)
                if b >= 1:
                    layer3(b - 1)
                layer1_half(b, 1)
                if b >= 1:
                    last_dot(b - 1)
            layer2(BLOCKS - 1)
            dots_to_rows(BLOCKS - 2)
            dot_products(BLOCKS - 1)
            layer3(BLOCKS - 1)
            last_dot(BLOCKS - 1)
            dots_to_rows(BLOCKS - 1)


INPUTS = ["r_user", "r_item", "L0_rec_user_emb", "L0_rec_item_emb", "L0_rec_cw1", "L0_rec_cw2",
          "L0_rec_dW1", "L0_rec_db1", "L0_rec_dW2", "L0_rec_db2", "L0_rec_dW3", "L0_rec_db3",
          "L0_rec_Wo", "L0_rec_bo"]


def kernel(**inputs):
    import numpy as np
    import concourse.bacc as bacc
    from concourse.bass_utils import run_bass_kernel_spmd

    nc = bacc.Bacc("TRN2", target_bir_lowering=False, num_devices=1)
    arrays = {name: np.ascontiguousarray(inputs[name]) for name in INPUTS}
    args = [nc.dram_tensor(name, a.shape, mybir.dt.from_np(a.dtype), kind="ExternalInput").ap()
            for name, a in arrays.items()]
    batch = arrays["r_user"].shape[0]
    scores = nc.dram_tensor("scores", (batch,), mybir.dt.float32, kind="ExternalOutput").ap()
    recommender(nc, *args, scores)
    ran = run_bass_kernel_spmd(nc, [arrays], core_ids=[0])
    return ran.results[0]["scores"]
```

```python
from contextlib import ExitStack

import concourse.bass as bass
from concourse import mybir

P = 128


def recommender(nc, user_ids, item_ids, user_emb, item_emb, cw1, cw2,
                dW1, db1, dW2, db2, dW3, db3, Wo, bo, scores):
    f32, f32r, i32 = mybir.dt.float32, mybir.dt.float32r, mybir.dt.int32
    ALU, ACT = mybir.AluOpType, mybir.ActivationFunctionType

    BATCH = user_ids.shape[0]
    HALF = user_emb.shape[1]
    D = 2 * HALF
    H1, H2, H3 = dW1.shape[1], dW2.shape[1], dW3.shape[1]
    TILES = BATCH // P
    S = 2
    N = S * P
    BLOCKS = TILES // S
    CH = HALF // P
    C1 = D // P
    C2 = H1 // P
    UNITS = 2 * BLOCKS
    TABLES = (user_emb, item_emb)
    DOTS = 3
    WARM_UP = 14
    Q = 32

    with ExitStack() as ctx:
        def sb(name, shape, dt=f32):
            return ctx.enter_context(nc.sbuf_tensor(name, shape, dt))

        def psum(name):
            return ctx.enter_context(nc.psum_tensor(name, [P, 512], f32))

        def sem(name):
            return ctx.enter_context(nc.semaphore(name))

        ids = sb("ids", [P, 2, TILES], i32)
        wrap = sb("wrap", [P, 2, TILES])
        wrapped = sb("wrapped", [P, 2, TILES])
        row_ids = sb("row_ids", [P, 2, TILES], i32)
        x = sb("x", [P, UNITS, S, HALF])
        xT = sb("xT", [P, UNITS, CH, N])
        xT_hi = sb("xT_hi", [P, UNITS, CH, N], f32r)
        xT_lo = sb("xT_lo", [P, UNITS, CH, N], f32r)
        w1 = sb("w1", [P, C1, H1])
        w1_hi = sb("w1_hi", [P, C1, H1], f32r)
        w1_lo = sb("w1_lo", [P, C1, H1], f32r)
        w2 = sb("w2", [P, C2, H2])
        w2_hi = sb("w2_hi", [P, C2, H2], f32r)
        w2_lo = sb("w2_lo", [P, C2, H2], f32r)
        w3 = sb("w3", [P, H3])
        R_DOT, R_B1, R_B2, R_B3, R_WOH = 0, DOTS * C1, DOTS * C1 + C2, DOTS * C1 + C2 + 1, DOTS * C1 + C2 + 2
        ROWS = R_WOH + 1
        vec_rows = sb("vec_rows", [P, P])
        vec = sb("vec", [P, ROWS])
        neg_b1 = sb("neg_b1", [P, C2])
        b2_folded = sb("b2_folded", [P, 1])
        bo_all = sb("bo_all", [P, 1])
        dot_w = sb("dot_w", [P, C1, Q])
        woh = sb("woh", [P, Q])
        ident = sb("ident", [P, P])
        h1_hi = sb("h1_hi", [P, 2, C2, N], f32r)
        h1_lo = sb("h1_lo", [P, 2, C2, N], f32r)
        h2 = sb("h2", [P, 2, N])
        h3 = sb("h3", [P, 2, N])
        dots = sb("dots", [P, 2, P])
        parts = sb("parts", [P, BLOCKS, S, 2, 4])
        both = sb("both", [P, TILES, 4])
        cross2 = sb("cross2", [P, TILES])
        cross = sb("cross", [P, TILES])
        score = sb("score", [P, TILES])

        tp = [psum("tp0"), psum("tp1")]
        h1p = [[psum(f"h1p{buf}{n}") for n in range(C2)] for buf in range(2)]
        h23_bank, dot_bank = psum("h23_bank"), psum("dot_bank")
        h2p, h3p = h23_bank[:, 0:N], h23_bank[:, N:N + P]
        last_part = h23_bank[:, N + P:N + P + S]
        dotp, dotTp = dot_bank[:, 0:P], dot_bank[:, P:2 * P]

        def dot_regions(b):
            return (tp[0][:, 0:P], tp[0][:, P:2 * P]) if b == BLOCKS - 1 else (dotp, dotTp)

        ids_landed = [sem("user_ids_landed"), sem("item_ids_landed")]
        vec_landed, w1_landed = sem("vec_landed"), sem("w1_landed")
        w2_landed, w3_landed, bo_landed = sem("w2_landed"), sem("w3_landed"), sem("bo_landed")
        x_landed = [sem(f"x_landed{k}") for k in range(UNITS)]
        wrap_done, ids_ready = sem("wrap_done"), sem("ids_ready")
        vec_zeroed = sem("vec_zeroed")
        zeroed, ident_zeroed, ident_ready = sem("zeroed"), sem("ident_zeroed"), sem("ident_ready")
        vecT_done, vec_ready, cols_ready = sem("vecT_done"), sem("vec_ready"), sem("cols_ready")
        fold_done, b2_ready = sem("fold_done"), sem("b2_ready")
        w1_hi_ready, w1_lo_ready = sem("w1_hi_ready"), sem("w1_lo_ready")
        w2_hi_ready, w2_lo_ready = sem("w2_hi_ready"), sem("w2_lo_ready")
        xT_done, hi_ready, whole_ready, lo_ready = sem("xT_done"), sem("hi_ready"), sem("whole_ready"), sem("lo_ready")
        h1_done, h1_hi_ready, h1_lo_ready = sem("h1_done"), sem("h1_hi_ready"), sem("h1_lo_ready")
        h2_done, h2_ready, h3_done = sem("h2_done"), sem("h2_ready"), sem("h3_done")
        h3a_ready, h3b_ready = sem("h3a_ready"), sem("h3b_ready")
        dots_done, dots_ready, dotsT_done, parts_ready = sem("dots_done"), sem("dots_ready"), sem("dotsT_done"), sem("parts_ready")
        both_ready, cross2_ready, cross_ready, score_ready = sem("both_ready"), sem("cross2_ready"), sem("cross_ready"), sem("score_ready")
        last_dots_done, last_part_done, stored = sem("last_dots_done"), sem("last_part_done"), sem("stored")

        block = ctx.enter_context(nc.Block())

        @block.sync
        def _(sp):
            sp.dma_start(ids[:, 0, :], user_ids.rearrange("(p t) -> p t", t=TILES)).then_inc(ids_landed[0], 16)
            sp.dma_start(ids[:, 1, :], item_ids.rearrange("(p t) -> p t", t=TILES)).then_inc(ids_landed[1], 16)
            sp.dma_start(w1[:, :, :], dW1.rearrange("(c p) n -> p c n", p=P)).then_inc(w1_landed, 16)
            row = lambda v: v.rearrange("(r n) -> r n", n=P)
            sp.wait_ge(vec_zeroed, 1)
            sp.dma_start(vec_rows[R_B1:R_B2, :], row(db1)).then_inc(vec_landed, 16)
            sp.dma_start(vec_rows[R_B2:R_B3, :], row(db2)).then_inc(vec_landed, 16)
            sp.dma_start(vec_rows[R_DOT:R_DOT + C1, :], row(cw1)).then_inc(vec_landed, 16)
            sp.dma_start(vec_rows[R_DOT + C1:R_DOT + 2 * C1, :], row(cw2)).then_inc(vec_landed, 16)
            sp.dma_start(vec_rows[R_DOT + 2 * C1:R_B1, :], Wo[0:D, :].rearrange("(r n) o -> r (n o)", n=P)).then_inc(vec_landed, 16)
            sp.dma_start(vec_rows[R_B3:R_WOH, :].rearrange("a (r n) -> a r n", n=H3),
                         db3.rearrange("(a r n) -> a r n", a=1, r=1).to_broadcast([1, P // H3, H3])).then_inc(vec_landed, 16)
            sp.dma_start(vec_rows[R_WOH:ROWS, 0:H3], Wo[D:D + H3, :].rearrange("(r n) o -> r (n o)", n=H3)).then_inc(vec_landed, 16)
            sp.dma_start(w2[:, :, :], dW2.rearrange("(c p) n -> p c n", p=P)).then_inc(w2_landed, 16)
            sp.dma_start(w3[:, :], dW3).then_inc(w3_landed, 16)
            sp.dma_start(bo_all[:, :], bo.rearrange("(a n) -> a n", a=1).to_broadcast([P, 1])).then_inc(bo_landed, 16)
            sp.wait_ge(score_ready, 2)
            sp.dma_start(scores.rearrange("(p t) -> p t", t=TILES), score[:, :]).then_inc(stored, 16)
            sp.wait_ge(stored, 16)

        @block.gpsimd
        def _(pool):
            pool.memset(ident[:, :], 0.0).then_inc(ident_zeroed, 1)
            pool.wait_ge(ident_zeroed, 1)
            pool.affine_select(out=ident[:, :], in_=ident[:, :], compare_op=ALU.not_equal, fill=1.0,
                               base=0, pattern=[[-1, P]], channel_multiplier=1).then_inc(ident_ready, 1)
            for k in range(UNITS):
                if k < 2:
                    pool.wait_ge(ids_ready, k + 1)
                for s in range(S):
                    t = (k // 2) * S + s
                    pool.indirect_dma_start(
                        out=x[:, k, s, :], out_offset=None, in_=TABLES[k % 2],
                        in_offset=bass.IndirectOffsetOnAxis(ap=row_ids[:, k % 2, t:t + 1], axis=0),
                    ).then_inc(x_landed[k], 16)

        @block.scalar
        def _(act):
            act.preload_act_table(ACT.Relu)
            act.wait_ge(w1_landed, 16)
            nc.scalar.activation(w1_hi[:, :, :], w1[:, :, :], ACT.Copy).then_inc(w1_hi_ready, 1)

            def hi_of(k):
                act.wait_ge(xT_done, k + 1)
                nc.scalar.activation(xT_hi[:, k, :, :], tp[k % 2][:, :], ACT.Copy).then_inc(hi_ready, 1)

            def whole_of(k):
                act.wait_ge(lo_ready, k + 1)
                nc.scalar.activation(xT[:, k, :, :], tp[k % 2][:, :], ACT.Copy).then_inc(whole_ready, 1)

            def keep_h2(b):
                act.wait_ge(h2_done, b + 1)
                if b == 0:
                    act.wait_ge(b2_ready, 1)
                if b >= 2:
                    act.wait_ge(h3_done, b - 1)
                nc.scalar.activation(h2[:, b % 2, :], h2p[:, 0:N], ACT.Relu, bias=b2_folded[:, 0:1]).then_inc(h2_ready, 1)

            def keep_h3_first(b):
                act.wait_ge(h3_done, b + 1)
                if b == 0:
                    act.wait_ge(zeroed, 4)
                if b >= 2:
                    act.wait_ge(dots_done, b - 1)
                nc.scalar.activation(h3[0:H3, b % 2, 0:P], h3p[0:H3, 0:P], ACT.Relu,
                                     bias=vec[0:H3, R_B3:R_B3 + 1]).then_inc(h3a_ready, 1)

            def keep_dots(b):
                if b == BLOCKS - 1:
                    act.wait_ge(last_dots_done, 1)
                else:
                    act.wait_ge(dots_done, b + 1)
                if b >= 2:
                    act.wait_ge(dotsT_done, b - 1)
                nc.scalar.activation(dots[:, b % 2, :], dot_regions(b)[0], ACT.Copy).then_inc(dots_ready, 1)

            hi_of(0)
            act.wait_ge(w2_landed, 16)
            nc.scalar.activation(w2_hi[:, :, :], w2[:, :, :], ACT.Copy).then_inc(w2_hi_ready, 1)
            whole_of(0)
            for b in range(BLOCKS):
                if b >= 2:
                    keep_dots(b - 2)
                hi_of(2 * b + 1)
                if b >= 1:
                    keep_h2(b - 1)
                whole_of(2 * b + 1)
                if b + 1 < BLOCKS:
                    hi_of(2 * b + 2)
                if b >= 1:
                    keep_h3_first(b - 1)
                if b + 1 < BLOCKS:
                    whole_of(2 * b + 2)
            keep_dots(BLOCKS - 2)
            keep_dots(BLOCKS - 1)
            keep_h2(BLOCKS - 1)
            keep_h3_first(BLOCKS - 1)

        @block.vector
        def _(dve):
            nc.vector.memset(vec_rows[:, :], 0.0).then_inc(vec_zeroed, 1)
            nc.vector.memset(dot_w[:, :, :], 0.0).then_inc(zeroed, 1)
            nc.vector.memset(woh[:, :], 0.0).then_inc(zeroed, 1)
            for buf in range(2):
                nc.vector.memset(h3[H3:P, buf, :], 0.0).then_inc(zeroed, 1)
            for table in range(2):
                rows = TABLES[table].shape[0]
                dve.wait_ge(ids_landed[table], 16)
                nc.vector.tensor_scalar(wrap[:, table, :], ids[:, table, :], 0.0, float(rows),
                                        ALU.is_lt, ALU.mult).then_inc(wrap_done, 1)
                dve.wait_ge(wrap_done, 2 * table + 1)
                nc.vector.tensor_tensor(wrapped[:, table, :], wrap[:, table, :], ids[:, table, :], ALU.add).then_inc(wrap_done, 1)
                dve.wait_ge(wrap_done, 2 * table + 2)
                nc.vector.tensor_scalar(row_ids[:, table, :], wrapped[:, table, :], 0.0, float(rows - 1),
                                        ALU.max, ALU.min).then_inc(ids_ready, 1)

            def lo_of(k):
                dve.wait_ge(hi_ready, k + 1)
                nc.vector.tensor_tensor(xT_lo[:, k, :, :], tp[k % 2][:, :].rearrange("p (c n) -> p c n", c=CH),
                                        xT_hi[:, k, :, :].bitcast(f32), ALU.subtract).then_inc(lo_ready, 1)

            dve.wait_ge(w1_hi_ready, 1)
            nc.vector.tensor_tensor(w1_lo[:, :, :], w1[:, :, :], w1_hi[:, :, :].bitcast(f32), ALU.subtract).then_inc(w1_lo_ready, 1)
            dve.wait_ge(vecT_done, 1)
            nc.vector.tensor_copy(vec[:, :], h2p[:, 0:ROWS]).then_inc(vec_ready, 1)
            dve.wait_ge(vec_ready, 1)
            dve.wait_ge(zeroed, 4)
            nc.vector.tensor_copy(dot_w[:, :, 0:DOTS],
                                  vec[:, R_DOT:R_B1].rearrange("p (i c) -> p c i", c=C1)).then_inc(cols_ready, 1)
            nc.vector.tensor_copy(woh[:, DOTS:DOTS + 1], vec[:, R_WOH:ROWS]).then_inc(cols_ready, 1)
            nc.vector.tensor_scalar(neg_b1[:, :], vec[:, R_B1:R_B2], -1.0, None, ALU.mult).then_inc(cols_ready, 1)
            dve.wait_ge(cols_ready, 3)

            lo_of(0)
            dve.wait_ge(w2_hi_ready, 1)
            nc.vector.tensor_tensor(w2_lo[:, :, :], w2[:, :, :], w2_hi[:, :, :].bitcast(f32), ALU.subtract).then_inc(w2_lo_ready, 1)

            def keep_h1(b):
                for n in range(C2):
                    dve.wait_ge(h1_done, C2 * b + n + 1)
                    if b >= 2:
                        dve.wait_ge(h2_done, b - 1)
                    nc.vector.tensor_scalar(h1_hi[:, b % 2, n, :], h1p[b % 2][n][:, 0:N], neg_b1[:, n:n + 1], None,
                                            ALU.max).then_inc(h1_hi_ready, 1)
                    dve.wait_ge(h1_hi_ready, C2 * b + n + 1)
                    nc.vector.scalar_tensor_tensor(h1_lo[:, b % 2, n, :], h1p[b % 2][n][:, 0:N], neg_b1[:, n:n + 1],
                                                   h1_hi[:, b % 2, n, :].bitcast(f32),
                                                   ALU.max, ALU.subtract).then_inc(h1_lo_ready, 1)

            def keep_h3_second(b):
                dve.wait_ge(h3_done, b + 1)
                if b >= 2:
                    dve.wait_ge(dots_done, b - 1)
                nc.vector.tensor_scalar(h3[0:H3, b % 2, P:N], h3p[H3:P, 0:P], vec[H3:P, R_B3:R_B3 + 1], 0.0,
                                        ALU.add, ALU.max).then_inc(h3b_ready, 1)

            def keep_parts(b):
                dve.wait_ge(dotsT_done, b + 1)
                nc.vector.tensor_copy(parts[:, b, :, :, :],
                                      dot_regions(b)[1].rearrange("p (s h q) -> p s h q", s=S, h=2)[:, :, :, 0:4]).then_inc(parts_ready, 1)

            lo_of(1)
            dve.wait_ge(fold_done, 1)
            nc.vector.tensor_tensor(b2_folded[:, :], h3p[:, 0:1], vec[:, R_B2:R_B3], ALU.add).then_inc(b2_ready, 1)
            for b in range(BLOCKS):
                if b >= 2:
                    keep_parts(b - 2)
                if b >= 1:
                    lo_of(2 * b + 1)
                if b >= 1:
                    keep_h3_second(b - 1)
                if b + 1 < BLOCKS:
                    lo_of(2 * b + 2)
                keep_h1(b)
            keep_parts(BLOCKS - 2)
            keep_parts(BLOCKS - 1)
            dve.wait_ge(parts_ready, BLOCKS)
            of_tile = parts[:, :, :, :, :].rearrange("p b s h i -> p (b s) h i")
            nc.vector.tensor_tensor(both[:, :, :], of_tile[:, :, 0, :], of_tile[:, :, 1, :], ALU.add).then_inc(both_ready, 1)
            dve.wait_ge(both_ready, 1)
            nc.vector.scalar_tensor_tensor(cross2[:, :], both[:, :, 1], 1.0, both[:, :, 2], ALU.add, ALU.mult).then_inc(cross2_ready, 1)
            keep_h3_second(BLOCKS - 1)
            dve.wait_ge(cross2_ready, 1)
            nc.vector.scalar_tensor_tensor(cross[:, :], both[:, :, 0], 1.0, cross2[:, :], ALU.add, ALU.mult).then_inc(cross_ready, 1)
            dve.wait_ge(cross_ready, 1)
            dve.wait_ge(bo_landed, 16)
            nc.vector.scalar_tensor_tensor(score[:, :], both[:, :, 3], bo_all[:, 0:1], cross[:, :], ALU.add, ALU.add).then_inc(score_ready, 1)
            dve.wait_ge(last_part_done, 1)
            dve.wait_ge(score_ready, 1)
            nc.vector.tensor_tensor(score[:, TILES - S:TILES], score[:, TILES - S:TILES], last_part, ALU.add).then_inc(score_ready, 1)

        @block.tensor
        def _(pe):
            mm = nc.tensor.matmul

            def vectors_to_columns():
                pe.wait_ge(vec_landed, 16 * 7)
                nc.tensor.transpose(h2p[:, 0:P], vec_rows[:, :], ident[:, :]).then_inc(vecT_done, 1)

            def fold_b1():
                pe.wait_ge(vec_ready, 1)
                pe.wait_ge(w2_landed, 16)
                for c in range(C2):
                    last = mm(h3p, w2[:, c, :], vec[:, R_B1 + c:R_B1 + c + 1].to_broadcast([P, P]), start=(c == 0), stop=(c == C2 - 1))
                last.then_inc(fold_done, 1)

            def transpose_unit(k):
                pe.wait_ge(x_landed[k], 16 * S)
                if k >= 2:
                    pe.wait_ge(whole_ready, k - 1)
                for s in range(S):
                    for c in range(CH):
                        last = nc.tensor.transpose(tp[k % 2][:, c * N + s * P:c * N + (s + 1) * P],
                                                   x[:, k, s, c * P:(c + 1) * P], ident[:, :])
                last.then_inc(xT_done, 1)

            def layer1_half(b, table):
                k = 2 * b + table
                pe.wait_ge(hi_ready, k + 1)
                for n in range(C2):
                    if table == 0 and n == C2 - 1 and b == 0:
                        transpose_unit(1)
                    if table == 0 and b >= 2:
                        pe.wait_ge(h1_lo_ready, C2 * (b - 2) + n + 1)
                    cols = slice(n * P, (n + 1) * P)
                    out = h1p[b % 2][n][:, 0:N]
                    for c in range(CH):
                        wc = table * CH + c
                        mm(out, w1_hi[:, wc, cols], xT_hi[:, k, c, :], start=(wc == 0), stop=False)
                        mm(out, w1_lo[:, wc, cols], xT_hi[:, k, c, :], start=False, stop=False)
                    pe.wait_ge(lo_ready, k + 1)
                    for c in range(CH):
                        wc = table * CH + c
                        last = mm(out, w1_hi[:, wc, cols], xT_lo[:, k, c, :], start=False, stop=(wc == C1 - 1))
                    if table == 1:
                        last.then_inc(h1_done, 1)

            def layer2_part(b, c):
                if b == 0:
                    pe.wait_ge(w2_lo_ready, 1)
                    pe.wait_ge(b2_ready, 1)
                else:
                    pe.wait_ge(h3a_ready, b)
                    pe.wait_ge(h3b_ready, b)
                pe.wait_ge(h1_hi_ready, C2 * b + c + 1)
                mm(h2p, w2_hi[:, c, :], h1_hi[:, b % 2, c, :], start=(c == 0), stop=False)
                mm(h2p, w2_lo[:, c, :], h1_hi[:, b % 2, c, :], start=False, stop=False)
                pe.wait_ge(h1_lo_ready, C2 * b + c + 1)
                last = mm(h2p, w2_hi[:, c, :], h1_lo[:, b % 2, c, :], start=False, stop=(c == C2 - 1))
                if c == C2 - 1:
                    last.then_inc(h2_done, 1)

            def dot_products(b):
                if b == 0:
                    pe.wait_ge(cols_ready, 3)
                elif b < BLOCKS - 1:
                    pe.wait_ge(parts_ready, b)
                pe.wait_ge(whole_ready, 2 * b + 2)
                for c in range(CH):
                    for s in range(S):
                        for table in range(2):
                            q = Q * (2 * s + table)
                            last = mm(dot_regions(b)[0][q:q + Q, :], dot_w[:, table * CH + c, :],
                                      xT[:, 2 * b + table, c, s * P:(s + 1) * P],
                                      start=(c == 0), stop=(c == CH - 1 and (table == 1 or b == BLOCKS - 1)))
                if b == BLOCKS - 1:
                    last.then_inc(last_dots_done, 1)

            def layer3(b):
                if b == 0:
                    pe.wait_ge(w3_landed, 16)
                pe.wait_ge(h2_ready, b + 1)
                for s in range(S):
                    last = mm(h3p[s * H3:(s + 1) * H3, 0:P], w3[:, :], h2[:, b % 2, s * P:(s + 1) * P], start=True, stop=True)
                last.then_inc(h3_done, 1)

            def last_dot(b):
                pe.wait_ge(h3a_ready, b + 1)
                pe.wait_ge(h3b_ready, b + 1)
                for s in range(S):
                    q = Q * 2 * s
                    last = mm(dotp[q:q + Q, 0:P], woh[:, :], h3[:, b % 2, s * P:(s + 1) * P], start=False, stop=True)
                last.then_inc(dots_done, 1)

            def dots_to_rows(b):
                pe.wait_ge(dots_ready, b + 1)
                nc.tensor.transpose(dot_regions(b)[1], dots[:, b % 2, :], ident[:, :]).then_inc(dotsT_done, 1)

            def keep_warm(n):
                for _ in range(n):
                    mm(dotp, ident[:, :], ident[:, :], start=True, stop=True)

            pe.wait_ge(ident_ready, 1)
            keep_warm(WARM_UP)
            vectors_to_columns()
            transpose_unit(0)
            keep_warm(2)
            pe.wait_ge(w1_lo_ready, 1)
            for b in range(BLOCKS):
                layer1_half(b, 0)
                if b >= 2:
                    dots_to_rows(b - 2)
                if b == 0:
                    fold_b1()
                else:
                    transpose_unit(2 * b + 1)
                    for c in range(C2):
                        layer2_part(b - 1, c)
                    dot_products(b - 1)
                if b + 1 < BLOCKS:
                    transpose_unit(2 * b + 2)
                if b >= 1:
                    layer3(b - 1)
                layer1_half(b, 1)
                if 1 <= b < BLOCKS - 1:
                    last_dot(b - 1)
            last_dot(BLOCKS - 2)
            layer2_part(BLOCKS - 1, 0)
            dot_products(BLOCKS - 1)
            layer2_part(BLOCKS - 1, 1)
            dots_to_rows(BLOCKS - 2)
            dots_to_rows(BLOCKS - 1)
            layer3(BLOCKS - 1)
            pe.wait_ge(h3a_ready, BLOCKS)
            pe.wait_ge(h3b_ready, BLOCKS)
            for s in range(S):
                last = mm(last_part[:, s:s + 1], h3[:, (BLOCKS - 1) % 2, s * P:(s + 1) * P], woh[:, DOTS:DOTS + 1], start=True, stop=True)
            last.then_inc(last_part_done, 1)


INPUTS = ["r_user", "r_item", "L0_rec_user_emb", "L0_rec_item_emb", "L0_rec_cw1", "L0_rec_cw2",
          "L0_rec_dW1", "L0_rec_db1", "L0_rec_dW2", "L0_rec_db2", "L0_rec_dW3", "L0_rec_db3",
          "L0_rec_Wo", "L0_rec_bo"]


def kernel(**inputs):
    import numpy as np
    import concourse.bacc as bacc
    from concourse.bass_utils import run_bass_kernel_spmd

    nc = bacc.Bacc("TRN2", target_bir_lowering=False, num_devices=1)
    arrays = {name: np.ascontiguousarray(inputs[name]) for name in INPUTS}
    args = [nc.dram_tensor(name, a.shape, mybir.dt.from_np(a.dtype), kind="ExternalInput").ap()
            for name, a in arrays.items()]
    batch = arrays["r_user"].shape[0]
    scores = nc.dram_tensor("scores", (batch,), mybir.dt.float32, kind="ExternalOutput").ap()
    recommender(nc, *args, scores)
    ran = run_bass_kernel_spmd(nc, [arrays], core_ids=[0])
    return ran.results[0]["scores"]
```
